# Optimizing a Trainium2 kernel written in Bass

```python
import numpy as np
import jax
import jax.numpy as jnp

def _softmax(x, axis=-1):
    return jax.nn.softmax(x, axis=axis)

def _gelu(x):
    return jax.nn.gelu(x, approximate=True)

def _silu(x):
    return jax.nn.silu(x)

def _sigmoid(x):
    return jax.nn.sigmoid(x)

def _layernorm(x, axis=-1, eps=1e-05):
    m = jnp.mean(x, axis=axis, keepdims=True)
    v = jnp.var(x, axis=axis, keepdims=True)
    return (x - m) / jnp.sqrt(v + eps)

def _scatter_add(tgt, idx, src, axis=0):
    return tgt.at[idx].add(src)

def _segment_sum(src, seg, n):
    return jax.ops.segment_sum(src, seg, n)
kernel_name = 'mk_adj_resnorm_d1_adj_r2_6e13eb'

def setup_inputs(seed: int=0):
    np.random.seed(seed)
    _w = jnp.asarray

    def _rec_inputs():
        import jax
        import jax.numpy as jnp
        _gk = jax.random.key(seed)
        x = -0.0002928 + 1 * jax.random.normal(jax.random.fold_in(_gk, 1), (4096, 256), jnp.float32)
        _a = jax.random.bernoulli(jax.random.fold_in(_gk, 2), 0.000976562, (4096, 4096))
        _a = jnp.logical_or(_a, jnp.swapaxes(_a, -1, -2))
        _a = jnp.logical_or(_a, jnp.eye(4096, dtype=bool))
        adj = _a.astype(jnp.int32)
        return (x, adj)
    x, adj = _rec_inputs()

    def _L0_gnn_setup():
        import jax, jax.numpy as jnp
        import numpy as np
        N = 4096
        IN_F = 256
        OUT_F = 256
        ALPHA = 0.2
        NEG_INF = -9000000000000000.0
        key = jax.random.key(seed)
        k1, k2, k3, k4, k5 = jax.random.split(key, 5)
        x = jax.random.normal(k1, (N, IN_F), dtype=jnp.float32)
        adj = jax.random.randint(k2, (N, N), 0, 2, dtype=jnp.int32)
        W = jax.random.normal(k3, (OUT_F, IN_F), dtype=jnp.float32) / np.sqrt(IN_F)
        a1 = jax.random.normal(k4, (OUT_F,), dtype=jnp.float32) / np.sqrt(2 * OUT_F)
        a2 = jax.random.normal(k5, (OUT_F,), dtype=jnp.float32) / np.sqrt(2 * OUT_F)
        return {'x': x, 'adj': adj, 'W': W, 'a1': a1, 'a2': a2}
    _L0_gnn_all = _L0_gnn_setup()
    _L0_gnn_in = {k: v for k, v in _L0_gnn_all.items() if k in ('W', 'a1', 'a2')}
    del _L0_gnn_all
    return {'x': x, 'adj': adj, 'L0_gnn_W': _L0_gnn_in['W'], 'L0_gnn_a1': _L0_gnn_in['a1'], 'L0_gnn_a2': _L0_gnn_in['a2']}

def reference(x, adj, L0_gnn_W, L0_gnn_a1, L0_gnn_a2):
    import jax
    import jax.numpy as jnp

    def _L0_gnn_ref(x, adj, W, a1, a2):
        import jax, jax.numpy as jnp
        import numpy as np
        N = 4096
        IN_F = 256
        OUT_F = 256
        ALPHA = 0.2
        NEG_INF = -9000000000000000.0
        h = x @ W.T
        src = h @ a1
        dst = h @ a2
        e = jax.nn.leaky_relu(src[:, None] + dst[None, :], negative_slope=ALPHA)
        e = jnp.where(adj == 0, jnp.float32(NEG_INF), e)
        attention = jax.nn.softmax(e, axis=1)
        h_prime = attention @ h
        return h_prime
    x = _layernorm(x + _L0_gnn_ref(x, adj, L0_gnn_W, L0_gnn_a1, L0_gnn_a2), axis=-1)
    return x

_drawn_inputs = setup_inputs


def setup_inputs(seed=0):
    import zlib

    import numpy as np

    out = dict(_drawn_inputs(seed))
    spreads = {}
    factors = {}
    for name, (base, spread) in spreads.items():
        noise = np.random.default_rng([zlib.crc32(name.encode()), seed]).standard_normal(out[name].shape)
        drawn = base * np.exp(spread * noise) if base else spread * noise
        out[name] = jnp.asarray(drawn.astype(out[name].dtype))
    for name, factor in factors.items():
        out[name] = (out[name] * factor).astype(out[name].dtype)
    return out
```

```python
import concourse.bass as bass
from concourse import mybir
from contextlib import ExitStack


fp32 = mybir.dt.float32
fp16 = mybir.dt.float16
bf16 = mybir.dt.bfloat16
i32 = mybir.dt.int32
ALU = mybir.AluOpType
ACT = mybir.ActivationFunctionType
AX = mybir.AxisListType

P = 128
ALPHA = 0.2
R = 4.0
BIG = 2.0 ** 62
SHIFT = 10.0
EPS = 1e-5
HTOP = 2.0 ** 14
BANK = 512
PERIOD = 6


def gat_layer(nc, x, adj, W, a1, a2, out):
    N, F = x.shape
    NT = N // P
    KB = F // P
    NH = 2
    HC = N // NH
    NC = 4
    CC = N // NC
    CB = CC // P
    RC = 3
    HG = CC // F
    NG = NT // HG
    NS = NC - 1
    LOOPS = (NT - 3) // PERIOD
    PEELED = range(LOOPS * PERIOD + 1, NT)

    adj_v = adj.rearrange("(t p) (h c) -> t p h c", p=P, h=NH)
    x_v = x.rearrange("(t p) f -> p t f", p=P)
    out_v = out.rearrange("(t p) f -> t p f", p=P)

    ctx = ExitStack()
    with ctx:
        def sb(name, shape, dt):
            return ctx.enter_context(nc.sbuf_tensor(name, shape, dt))

        def sem(name):
            return ctx.enter_context(nc.semaphore(name))

        x_sb = sb("x_sb", [P, NT, F], fp32)
        h_hi = sb("h_hi", [P, NT, F], fp16)
        h_lo = sb("h_lo", [P, NT, F], fp16)
        h_full = sb("h_full", [P, CB, F], fp32)
        d_row = sb("d_row", [P, N], fp32)
        s_col = sb("s_col", [P, NT], fp32)
        ident = sb("ident", [P, P], fp32)
        ones = sb("ones", [P, P], fp32)
        half = sb("half", [P, 1], fp32)
        w_sb = sb("w_sb", [P, KB, F], fp32)
        wT = sb("wT", [P, KB, F], fp32)
        a12 = sb("a12", [P, KB, 2], fp32)
        w12 = sb("w12", [P, KB, 2], fp32)
        d_col = sb("d_col", [P, NT], fp32)
        xT = sb("xT", [P, KB, N], fp32)
        mags = sb("mags", [P, NG + 1], fp32)
        mag2 = sb("mag2", [P, 2], fp32)
        top2 = sb("top2", [P, 2], fp32)
        bound = sb("bound", [P, 1], fp32)
        pow2 = sb("pow2", [P, 1], fp32)
        rpow2 = sb("rpow2", [P, 1], fp32)
        sigma = sb("sigma", [P, 1], fp32)
        adj_sb = sb("adj_sb", [P, 2 * NH, HC], i32)
        w = sb("w", [P, 2, N], fp32)
        half_ring = RC * CC // 2
        e_full = xT[:, 0, 0:CC]
        e_hi = xT[:, 0, CC:CC + half_ring].bitcast(fp16).rearrange("p (r c) -> p r c", r=RC)
        e_lo = xT[:, 1, 0:half_ring].bitcast(fp16).rearrange("p (r c) -> p r c", r=RC)
        wmax = sb("wmax", [P, 2, NH], fp32)
        negmax = sb("negmax", [P, 2], fp32)
        den = sb("den", [P, 3, NH], fp32)
        dsum = sb("dsum", [P, 2], fp32)
        rden = sb("rden", [P, 2], fp32)
        y = sb("y", [P, 2, F], fp32)
        stats = sb("stats", [P, 2, 6], fp32)
        mv = sb("mv", [P, 2, 2], fp32)
        veps = sb("veps", [P, 2], fp32)
        rstd = sb("rstd", [P, 2], fp32)
        o_sb = sb("o_sb", [P, 2, F], fp32)
        diag = w[:, 1, :].rearrange("p (t q) -> p t q", t=NT)

        tp = [ctx.enter_context(nc.psum_tensor(f"tp{r}", [P, CC], fp32)) for r in range(RC)]
        acc = [ctx.enter_context(nc.psum_tensor(f"acc{r}", [P, BANK], fp32)) for r in range(2)]

        w_in = sem("w_in")
        a_in = sem("a_in")
        x_in = [sem(f"x_in{g}") for g in range(NG)]
        consts = sem("consts")
        const_step = sem("const_step")
        wT_ready = sem("wT_ready")
        wT_copied = sem("wT_copied")
        w12_ready = sem("w12_ready")
        w12_copied = sem("w12_copied")
        xT_ready = sem("xT_ready")
        xT_even = sem("xT_even")
        xT_odd = sem("xT_odd")
        sd_ready = sem("sd_ready")
        sd_copied = sem("sd_copied")
        diag_done = sem("diag_done")
        drow_ready = sem("drow_ready")
        drow_copied = sem("drow_copied")
        mag_step = sem("mag_step")
        mag_ready = sem("mag_ready")
        top_ready = sem("top_ready")
        sigma_ready = sem("sigma_ready")
        h_ready = sem("h_ready")
        hhi_done = sem("hhi_done")
        hlo_done = sem("hlo_done")
        adj_in = [sem(f"adj_in{r}") for r in range(2 * NH)]
        u_done = sem("u_done")
        relu_done = sem("relu_done")
        v_done = sem("v_done")
        negmax_done = sem("negmax_done")
        exp_done = sem("exp_done")
        tp_done = sem("tp_done")
        hi_done = sem("hi_done")
        lo_done = sem("lo_done")
        prod_done = sem("prod_done")
        dve_step = sem("dve_step")
        y_done = sem("y_done")
        mv_done = sem("mv_done")
        veps_done = sem("veps_done")
        rstd_done = sem("rstd_done")
        norm_done = sem("norm_done")
        stored = [sem(f"stored{r}") for r in range(2)]

        block = ctx.enter_context(nc.Block())

        @block.sync
        def _(sp):
            sp.dma_start(w_sb[:], W.rearrange("(b p) k -> p b k", p=P)).then_inc(w_in, 16)
            with nc.allow_non_contiguous_dma(reason="2 x 256 numbers"):
                sp.dma_start(a12[:, :, 0], a1.rearrange("(b p) -> p b", p=P)).then_inc(a_in, 16)
                sp.dma_start(a12[:, :, 1], a2.rearrange("(b p) -> p b", p=P)).then_inc(a_in, 16)
            for g in range(NG):
                ts = slice(g * HG, (g + 1) * HG)
                sp.dma_start(x_sb[:, ts, :], x_v[:, ts, :]).then_inc(x_in[g], 16)

            def load(i, c, ring_used=True):
                for h in range(NH):
                    if ring_used:
                        sp.wait_ge(v_done, NH * PERIOD * i + NH * (c - 2) + h + 1)
                    r = NH * (c % 2) + h
                    sp.dma_start(adj_sb[:, r, :], adj_v[PERIOD * i + c, :, h, :]).then_inc(adj_in[r], 16)

            def store(i, c):
                sp.wait_ge(norm_done, PERIOD * i + c + 1)
                sp.dma_start(out_v[PERIOD * i + c, :, :], o_sb[:, c % 2, :]).then_inc(stored[c % 2], 16)

            load(0, 0, False)
            load(0, 1, False)
            load(0, 2)
            load(0, 3)
            with sp.Fori(0, LOOPS) as i:
                for c in range(1, PERIOD + 1):
                    load(i, c + 3)
                    store(i, c - 1)
            for t in PEELED:
                if t + 3 < NT:
                    load(0, t + 3)
                store(0, t - 1)
            store(0, NT - 1)
            for r in range(2):
                sp.wait_ge(stored[r], 16 * (NT // 2))

        @block.gpsimd
        def _(pool):
            nc.gpsimd.memset(ident[:], 0.0).then_inc(const_step, 1)
            pool.wait_ge(const_step, 1)
            nc.gpsimd.affine_select(out=ident[:], in_=ident[:], compare_op=ALU.not_equal, fill=1.0, base=0,
                                    pattern=[[-1, P]], channel_multiplier=1).then_inc(consts, 1)
            nc.gpsimd.memset(ones[:], 1.0).then_inc(consts, 1)
            nc.gpsimd.memset(half[:], -0.5).then_inc(consts, 1)
            pool.wait_ge(mag_ready, 1)
            nc.gpsimd.partition_all_reduce(top2[:], mag2[:], P, bass.bass_isa.ReduceOp.max).then_inc(top_ready, 1)

            def normalise(i, c, ring_used=True):
                r = c % 2
                pool.wait_ge(mv_done, PERIOD * i + c + 1)
                nc.gpsimd.nop(nofuse=True)
                nc.gpsimd.tensor_scalar(veps[:, r:r + 1], mv[:, r, 1:2], 1.0, EPS,
                                        ALU.mult, ALU.add).then_inc(veps_done, 1)
                pool.wait_ge(veps_done, PERIOD * i + c + 1)
                nc.gpsimd.tensor_tensor(rstd[:, r:r + 1], veps[:, r:r + 1], half[:],
                                        ALU.pow).then_inc(rstd_done, 1)
                pool.wait_ge(rstd_done, PERIOD * i + c + 1)
                if ring_used:
                    pool.wait_ge(stored[r], 16 * (PERIOD // 2) * i + 16 * (c // 2))
                nc.gpsimd.nop(nofuse=True)
                nc.gpsimd.tensor_scalar(o_sb[:, r, :], y[:, r, :], mv[:, r, 0:1], rstd[:, r:r + 1],
                                        ALU.subtract, ALU.mult).then_inc(norm_done, 1)

            for t in range(2):
                normalise(0, t, False)
            with pool.Fori(0, LOOPS) as i:
                for c in range(2, PERIOD + 2):
                    normalise(i, c)
            for t in range(LOOPS * PERIOD + 2, NT):
                normalise(0, t)

        @block.scalar
        def _(act):
            for g in range(1, NG, 2):
                act.wait_ge(xT_ready, g + 1)
                nc.scalar.copy(xT[:, :, g * HG * P:(g + 1) * HG * P],
                               tp[g % RC][:].rearrange("p (b n) -> p b n", b=KB)).then_inc(xT_odd, 1)
            for c in range(NC):
                act.wait_ge(drow_ready, c + 1)
                nc.scalar.activation(d_row[:, c * CC:(c + 1) * CC], tp[(NG + c) % RC][:], ACT.Copy,
                                     scale=(1 - ALPHA) / BIG).then_inc(drow_copied, 1)

            def relu(i, c, h, ring_used=True):
                if ring_used:
                    act.wait_ge(tp_done, NC * PERIOD * i + NC * (c - 2) + 2 * h + 2)
                    nc.scalar.nop(nofuse=True)
                nc.scalar.activation(w[:, c % 2, h * HC:(h + 1) * HC], d_row[:, h * HC:(h + 1) * HC], ACT.Relu,
                                     bias=s_col[:, bass.ds(PERIOD * i + c, 1)], scale=R).then_inc(relu_done, 1)

            def expo(i, c, h, ring_used=True):
                if h == 0:
                    act.wait_ge(negmax_done, PERIOD * i + c + 1)
                    if ring_used:
                        act.wait_ge(y_done, PERIOD * i + c - 2)
                v = w[:, c % 2, h * HC:(h + 1) * HC]
                nc.scalar.activation(v, v, ACT.Exp, bias=negmax[:, c % 2:c % 2 + 1], scale=BIG / R,
                                     accum_out=den[:, c % 3, h:h + 1]).then_inc(exp_done, 1)

            def high(i, c, k, ring_used=True):
                act.wait_ge(tp_done, NC * PERIOD * i + NC * c + k + 1)
                r = (NC * c + k) % RC
                if k == NC - 1:
                    if ring_used:
                        act.wait_ge(prod_done, NC * PERIOD * i + NC * c)
                    nc.scalar.copy(e_full, tp[r][:]).then_inc(hi_done, 1)
                else:
                    if ring_used:
                        act.wait_ge(prod_done, NC * PERIOD * i + NC * c + k - RC + 1)
                    nc.scalar.copy(e_hi[:, r, :], tp[r][:]).then_inc(hi_done, 1)

            act.wait_ge(drow_copied, NC)
            act.wait_ge(sd_copied, 2)
            relu(0, 0, 0, False)
            relu(0, 0, 1, False)
            relu(0, 1, 0, False)
            relu(0, 1, 1, False)
            act.wait_ge(sigma_ready, 1)
            for g in range(NG):
                act.wait_ge(h_ready, g + 1)
                nc.scalar.activation(h_hi[:, g * HG:(g + 1) * HG, :],
                                     tp[(NG + NC + g) % RC][:].rearrange("p (t f) -> p t f", t=HG),
                                     ACT.Copy, scale=sigma[:, 0:1]).then_inc(hhi_done, 1)
                if g == 2:
                    expo(0, 0, 0, False)
                if g == 4:
                    expo(0, 0, 1, False)

            def tile(i, c):
                t = c if type(i) is int else None
                high(i, c, 0, t != 0)
                if t is None or t + 2 < NT:
                    relu(i, c + 2, 0)
                high(i, c, 1, t != 0)
                if t is None or t + 1 < NT:
                    expo(i, c + 1, 0, t is None or t >= 2)
                high(i, c, 2, t != 0)
                if t is None or t + 1 < NT:
                    expo(i, c + 1, 1)
                high(i, c, 3, t != 0)
                if t is None or t + 2 < NT:
                    relu(i, c + 2, 1)

            tile(0, 0)
            tile(0, 1)
            for t in range(2, PERIOD + 1):
                tile(0, t)
            with act.Fori(1, LOOPS) as i:
                for c in range(1, PERIOD + 1):
                    tile(i, c)
            for t in PEELED:
                tile(0, t)

        @block.vector
        def _(dve):
            dve.wait_ge(wT_ready, 1)
            nc.vector.tensor_copy(wT[:], tp[0][:, 0:KB * F].rearrange("p (b f) -> p b f", b=KB)
                                  ).then_inc(wT_copied, 1)
            dve.wait_ge(w12_ready, 1)
            nc.vector.tensor_copy(w12[:], acc[0][:, 0:2 * KB].rearrange("p (b f) -> p b f", b=KB)
                                  ).then_inc(w12_copied, 1)
            for g in range(NG):
                dve.wait_ge(x_in[g], 16)
                nc.vector.tensor_reduce(mags[:, g:g + 1], x_sb[:, g * HG:(g + 1) * HG, :], AX.XY, ALU.max,
                                        apply_absolute_value=True).then_inc(mag_step, 1)
                if g % 2 == 0:
                    dve.wait_ge(xT_ready, g + 1)
                    nc.vector.tensor_copy(xT[:, :, g * HG * P:(g + 1) * HG * P],
                                          tp[g % RC][:].rearrange("p (b n) -> p b n", b=KB)
                                          ).then_inc(xT_even, 1)
            dve.wait_ge(sd_ready, 1)
            sd = acc[1][:, 0:2 * NT].rearrange("p (t k) -> p t k", k=2)
            nc.vector.tensor_copy(d_col[:], sd[:, :, 1]).then_inc(sd_copied, 1)
            nc.vector.tensor_scalar(s_col[:], sd[:, :, 0], R * (1 - ALPHA) / BIG, None, ALU.mult
                                    ).then_inc(sd_copied, 1)
            dve.wait_ge(sd_copied, 1)
            dve.wait_ge(consts, 3)
            nc.vector.tensor_tensor(diag, ident[:].unsqueeze(1).broadcast_to([P, NT, P]),
                                    d_col[:].unsqueeze(2).broadcast_to([P, NT, P]), ALU.mult
                                    ).then_inc(diag_done, 1)

            nc.vector.tensor_reduce(mag2[:, 1:2], w_sb[:], AX.XY, ALU.max,
                                    apply_absolute_value=True).then_inc(mag_step, 1)
            dve.wait_ge(mag_step, NG + 1)
            nc.vector.tensor_reduce(mag2[:, 0:1], mags[:, 0:NG], AX.X, ALU.max).then_inc(mag_ready, 1)
            dve.wait_ge(top_ready, 1)
            nc.vector.tensor_scalar(bound[:], top2[:, 0:1], top2[:, 1:2], float(F), ALU.mult, ALU.mult
                                    ).then_inc(mag_step, 1)
            dve.wait_ge(mag_step, NG + 2)
            nc.vector.tensor_scalar(rpow2[:], bound[:], 1e-30, None, ALU.max).then_inc(mag_step, 1)
            dve.wait_ge(mag_step, NG + 3)
            nc.vector.tensor_scalar(pow2[:].bitcast(i32), rpow2[:].bitcast(i32), 0x7F800000, None,
                                    ALU.bitwise_and).then_inc(mag_step, 1)
            dve.wait_ge(mag_step, NG + 4)
            nc.vector.reciprocal(rpow2[:], pow2[:]).then_inc(mag_step, 1)
            dve.wait_ge(mag_step, NG + 5)
            nc.vector.tensor_scalar(sigma[:], rpow2[:], HTOP, None, ALU.mult).then_inc(sigma_ready, 1)

            def edges(i, c, h):
                r = NH * (c % 2) + h
                dve.wait_ge(adj_in[r], 16 * (PERIOD // 2) * i + 16 * (c // 2 + 1))
                nc.vector.scalar_tensor_tensor(
                    out=adj_sb[:, r, :].bitcast(fp32), in0=adj_sb[:, r, :], scalar=0.0,
                    in1=d_row[:, h * HC:(h + 1) * HC], op0=ALU.is_equal, op1=ALU.subtract).then_inc(u_done, 1)

            def scores(i, c, h):
                r = NH * (c % 2) + h
                dve.wait_ge(u_done, NH * PERIOD * i + NH * c + h + 1)
                dve.wait_ge(relu_done, NH * PERIOD * i + NH * c + h + 1)
                if h:
                    dve.wait_ge(v_done, NH * PERIOD * i + NH * c + h)
                nc.vector.nop(nofuse=True)
                v = w[:, c % 2, h * HC:(h + 1) * HC]
                nc.vector.tensor_tensor_reduce(
                    out=v, in0=v, in1=adj_sb[:, r, :].bitcast(fp32), scale=1.0,
                    scalar=(wmax[:, c % 2, h - 1:h] if h else -3e38), op0=ALU.subtract, op1=ALU.max,
                    accum_out=wmax[:, c % 2, h:h + 1]).then_inc(v_done, 1)

            def row_max(i, c, ring_used=True):
                dve.wait_ge(v_done, NH * PERIOD * i + NH * (c + 1))
                if ring_used:
                    dve.wait_ge(exp_done, NH * PERIOD * i + NH * (c - 1))
                nc.vector.tensor_scalar(negmax[:, c % 2:c % 2 + 1], wmax[:, c % 2, NH - 1:NH], -BIG / R, SHIFT,
                                        ALU.mult, ALU.add).then_inc(negmax_done, 1)

            def low(i, c, k):
                dve.wait_ge(hi_done, NC * PERIOD * i + NC * c + k + 1)
                r = (NC * c + k) % RC
                nc.vector.tensor_tensor(e_lo[:, r, :], tp[r][:], e_hi[:, r, :], ALU.subtract
                                        ).then_inc(lo_done, 1)

            def residual(i, c, ring_used=True):
                r = c % 2
                step = 3 * PERIOD * i + 3 * c
                dve.wait_ge(prod_done, NC * PERIOD * i + NC * (c + 1))
                nc.vector.tensor_scalar(dsum[:, r:r + 1], den[:, c % 3, 0:1], den[:, c % 3, 1:2], sigma[:, 0:1],
                                        ALU.add, ALU.mult).then_inc(dve_step, 1)
                dve.wait_ge(dve_step, step + 1)
                nc.vector.reciprocal(rden[:, r:r + 1], dsum[:, r:r + 1]).then_inc(dve_step, 1)
                dve.wait_ge(dve_step, step + 2)
                if ring_used:
                    dve.wait_ge(norm_done, PERIOD * i + c - 1)
                nc.vector.scalar_tensor_tensor(
                    out=y[:, r, :], in0=acc[r][:, 0:F], scalar=rden[:, r:r + 1],
                    in1=x_sb[:, bass.ds(PERIOD * i + c, 1), :].rearrange("p t f -> p (t f)"),
                    op0=ALU.mult, op1=ALU.add).then_inc(y_done, 1)
                dve.wait_ge(y_done, PERIOD * i + c + 1)
                nc.vector.bn_stats(stats[:, r, :], y[:, r, :]).then_inc(dve_step, 1)
                dve.wait_ge(dve_step, step + 3)
                nc.vector.nop(nofuse=True)
                nc.vector.bn_aggr(mv[:, r, :], stats[:, r, :]).then_inc(mv_done, 1)

            dve.wait_ge(drow_copied, NC)
            edges(0, 0, 0)
            edges(0, 0, 1)
            scores(0, 0, 0)
            scores(0, 0, 1)
            row_max(0, 0, False)
            edges(0, 1, 0)
            scores(0, 1, 0)
            edges(0, 1, 1)
            for g in range(NG):
                dve.wait_ge(hhi_done, g + 1)
                hp = tp[(NG + NC + g) % RC][:].rearrange("p (t f) -> p t f", t=HG)
                if (g + 1) * HG > NS * CB:
                    b0 = g * HG - NS * CB
                    nc.vector.tensor_scalar(h_full[:, b0:b0 + HG, :], hp, sigma[:, 0:1], None, ALU.mult)
                nc.vector.scalar_tensor_tensor(
                    out=h_lo[:, g * HG:(g + 1) * HG, :], in0=hp, scalar=sigma[:, 0:1],
                    in1=h_hi[:, g * HG:(g + 1) * HG, :], op0=ALU.mult, op1=ALU.subtract).then_inc(hlo_done, 1)

            def tile(i, c):
                t = c if type(i) is int else None
                low(i, c, 0)
                if t is None or t + 1 < NT:
                    scores(i, c + 1, 1)
                    row_max(i, c + 1, t is None or t >= 1)
                low(i, c, 1)
                if t is None or t + 2 < NT:
                    edges(i, c + 2, 0)
                    scores(i, c + 2, 0)
                low(i, c, 2)
                if t != 0:
                    residual(i, c - 1, t is None or t >= 3)
                if t is None or t + 2 < NT:
                    edges(i, c + 2, 1)

            for t in range(PERIOD + 1):
                tile(0, t)
            with dve.Fori(1, LOOPS) as i:
                for c in range(1, PERIOD + 1):
                    tile(i, c)
            for t in PEELED:
                tile(0, t)
            residual(0, NT - 1)

        @block.tensor
        def _(pe):
            pe.wait_ge(consts, 3)
            pe.wait_ge(w_in, 16)
            pe.wait_ge(a_in, 32)
            for b in range(KB):
                for fb in range(KB):
                    last = nc.tensor.transpose(tp[0][:, b * F + fb * P:b * F + (fb + 1) * P],
                                               w_sb[:, fb, b * P:(b + 1) * P], ident[:])
            last.then_inc(wT_ready, 1)
            for b in range(KB):
                for fb in range(KB):
                    last = nc.tensor.matmul(acc[0][:, 2 * b:2 * b + 2], w_sb[:, fb, b * P:(b + 1) * P],
                                            a12[:, fb, :], start=(fb == 0), stop=(fb == KB - 1))
            last.then_inc(w12_ready, 1)
            pe.wait_ge(wT_copied, 1)

            for g in range(NG):
                pe.wait_ge(x_in[g], 16)
                if g >= RC:
                    before = g - RC
                    pe.wait_ge(xT_odd if before % 2 else xT_even, before // 2 + 1)
                for b in range(KB):
                    for u in range(HG):
                        last = nc.tensor.transpose(tp[g % RC][:, (b * HG + u) * P:(b * HG + u + 1) * P],
                                                   x_sb[:, g * HG + u, b * P:(b + 1) * P], ident[:])
                last.then_inc(xT_ready, 1)
            pe.wait_ge(w12_copied, 1)
            pe.wait_ge(xT_even, NG // 2)
            pe.wait_ge(xT_odd, NG // 2)
            for t in range(NT):
                for b in range(KB):
                    last = nc.tensor.matmul(acc[1][:, 2 * t:2 * t + 2], xT[:, b, t * P:(t + 1) * P],
                                            w12[:, b, :], start=(b == 0), stop=(b == KB - 1))
            last.then_inc(sd_ready, 1)
            pe.wait_ge(diag_done, 1)
            for c in range(NC):
                if c >= RC:
                    pe.wait_ge(drow_copied, c - RC + 1)
                for q in range(CC // BANK):
                    lo = c * CC + q * BANK
                    last = nc.tensor.matmul(tp[(NG + c) % RC][:, q * BANK:(q + 1) * BANK], ones[:],
                                            w[:, 1, lo:lo + BANK], start=True, stop=True)
                last.then_inc(drow_ready, 1)
            pe.wait_ge(drow_copied, NC)
            for g in range(NG):
                if g >= RC:
                    pe.wait_ge(hlo_done, g - RC + 1)
                for u in range(HG):
                    t = g * HG + u
                    for b in range(KB):
                        last = nc.tensor.matmul(tp[(NG + NC + g) % RC][:, u * F:(u + 1) * F],
                                                xT[:, b, t * P:(t + 1) * P], wT[:, b, :],
                                                start=(b == 0), stop=(b == KB - 1))
                last.then_inc(h_ready, 1)

            def flip(i, c, k, ring_used=True):
                if k % 2 == 0:
                    pe.wait_ge(exp_done, NH * PERIOD * i + NH * c + k // 2 + 1)
                if ring_used:
                    if (k - RC) % NC == NC - 1:
                        pe.wait_ge(hi_done, NC * PERIOD * i + NC * c + k - RC + 1)
                    else:
                        tiles, kk = (k - RC) // NC, (k - RC) % NC
                        pe.wait_ge(lo_done, NS * PERIOD * i + NS * (c + tiles) + kk + 1)
                r = (NC * c + k) % RC
                for b in range(CB):
                    j = k * CB + b
                    last = nc.tensor.transpose(tp[r][:, b * P:(b + 1) * P], w[:, c % 2, j * P:(j + 1) * P], ident[:])
                last.then_inc(tp_done, 1)

            def product(i, c, k, ring_used=True):
                r = (NC * c + k) % RC
                sums = acc[c % 2][:, 0:F]
                if k == 0 and ring_used:
                    pe.wait_ge(y_done, PERIOD * i + c - 1)
                if k < NS:
                    pe.wait_ge(lo_done, NS * PERIOD * i + NS * c + k + 1)
                    for b in range(CB):
                        j = k * CB + b
                        hi = e_hi[:, r, b * P:(b + 1) * P]
                        nc.tensor.matmul(sums, hi, h_hi[:, j, :], start=(j == 0), stop=False)
                        nc.tensor.matmul(sums, hi, h_lo[:, j, :], start=False, stop=False)
                        last = nc.tensor.matmul(sums, e_lo[:, r, b * P:(b + 1) * P], h_hi[:, j, :],
                                                start=False, stop=False)
                else:
                    pe.wait_ge(hi_done, NC * PERIOD * i + NC * c + k + 1)
                    for b in range(CB):
                        last = nc.tensor.matmul(sums, e_full[:, b * P:(b + 1) * P], h_full[:, b, :],
                                                start=False, stop=(b == CB - 1))
                last.then_inc(prod_done, 1)

            def tile(i, c):
                t = c if type(i) is int else None
                for k in range(NC):
                    if k + 2 < NC:
                        flip(i, c, k + 2, t != 0 or k + 2 >= RC)
                    elif t is None or t + 1 < NT:
                        flip(i, c + 1, k + 2 - NC)
                    product(i, c, k, t is None or t >= 2)

            pe.wait_ge(hlo_done, NG)
            flip(0, 0, 0, False)
            flip(0, 0, 1, False)
            for t in range(PERIOD + 1):
                tile(0, t)
            with pe.Fori(1, LOOPS) as i:
                for c in range(1, PERIOD + 1):
                    tile(i, c)
            for t in PEELED:
                tile(0, t)


_INS = ['x', 'adj', 'L0_gnn_W', 'L0_gnn_a1', 'L0_gnn_a2']


def kernel(**inputs):
    import numpy as _np
    import concourse.bacc as _bacc
    from concourse import mybir as _mybir
    from concourse.bass_utils import run_bass_kernel_spmd as _run

    nc = _bacc.Bacc("TRN2", target_bir_lowering=False, num_devices=1)
    arrays, args = {}, []
    for name in _INS:
        a = _np.ascontiguousarray(inputs[name])
        arrays[f"in_{name}_dram"] = a
        args.append(nc.dram_tensor(f"in_{name}_dram", a.shape, _mybir.dt.from_np(a.dtype), kind="ExternalInput").ap())
    shape = inputs['x'].shape
    out = nc.dram_tensor("out_0_dram", shape, _mybir.dt.float32, kind="ExternalOutput").ap()
    gat_layer(nc, *args, out)
    r = _run(nc, [arrays], core_ids=[0])
    return r.results[0]["out_0_dram"]
```

```python
import concourse.bass as bass
from concourse import mybir
from contextlib import ExitStack


fp32 = mybir.dt.float32
fp16 = mybir.dt.float16
bf16 = mybir.dt.bfloat16
i32 = mybir.dt.int32
ALU = mybir.AluOpType
ACT = mybir.ActivationFunctionType
AX = mybir.AxisListType

P = 128
ALPHA = 0.2
R = 4.0
BIG = 2.0 ** 62
SHIFT = 10.0
EPS = 1e-5
HTOP = 2.0 ** 14
BANK = 512
PERIOD = 6


def gat_layer(nc, x, adj, W, a1, a2, out):
    N, F = x.shape
    NT = N // P
    KB = F // P
    NH = 2
    HC = N // NH
    NC = 4
    CC = N // NC
    CB = CC // P
    RC = 3
    HG = CC // F
    NG = NT // HG
    GC = HG * P
    TP = 2
    NP = NT // TP
    LOOPS = (NT - 3) // PERIOD
    PEELED = range(LOOPS * PERIOD + 1, NT)

    adj_v = adj.rearrange("(t p) (h c) -> t p h c", p=P, h=NH)
    x_v = x.rearrange("(t p) f -> p t f", p=P)
    out_v = out.rearrange("(t p) f -> t p f", p=P)

    ctx = ExitStack()
    with ctx:
        def sb(name, shape, dt):
            return ctx.enter_context(nc.sbuf_tensor(name, shape, dt))

        def sem(name):
            return ctx.enter_context(nc.semaphore(name))

        x_sb = sb("x_sb", [P, NT, F], fp32)
        h_hi = sb("h_hi", [P, NT, F], fp16)
        h_lo = sb("h_lo", [P, NT, F], fp16)
        d_row = sb("d_row", [P, N], fp32)
        s_col = sb("s_col", [P, NT], fp32)
        ident = sb("ident", [P, P], fp32)
        powers = sb("powers", [P, 2], fp32)
        w_sb = sb("w_sb", [P, KB, F], fp32)
        wT = sb("wT", [P, KB, F + 1], fp32)
        a12 = sb("a12", [P, KB, 2], fp32)
        a2_rep = sb("a2_rep", [P, KB, P], fp32)
        w2_rep = sb("w2_rep", [P, KB, P], fp32)
        xT = sb("xT", [P, KB, N], fp32)
        mags = sb("mags", [P, NG + 1], fp32)
        mag2 = sb("mag2", [P, 2], fp32)
        top2 = sb("top2", [P, 2], fp32)
        bound = sb("bound", [P, 1], fp32)
        pow2 = sb("pow2", [P, 1], fp32)
        rpow2 = sb("rpow2", [P, 1], fp32)
        sigma = sb("sigma", [P, 1], fp32)
        adj_sb = sb("adj_sb", [P, 2 * NH, HC], i32)
        w = sb("w", [P, 2, N], fp32)
        half_ring = RC * CC // 2
        e_hi = xT[:, 0, 0:half_ring].bitcast(fp16).rearrange("p (r c) -> p r c", r=RC)
        e_lo = xT[:, 1, 0:half_ring].bitcast(fp16).rearrange("p (r c) -> p r c", r=RC)
        wmax = sb("wmax", [P, 2, NH], fp32)
        negmax = sb("negmax", [P, 2], fp32)
        den = sb("den", [P, 3, NH], fp32)
        dsum = sb("dsum", [P, 2], fp32)
        rden = sb("rden", [P, 2], fp32)
        y = sb("y", [P, 2, F], fp32)
        ysum = sb("ysum", [P, 2], fp32)
        nmean = sb("nmean", [P, 2], fp32)
        ysq = sb("ysq", [P, 2], fp32)
        unused = sb("unused", [P, 2, F], fp32)
        veps = sb("veps", [P, 2], fp32)
        rstd = sb("rstd", [P, 2], fp32)
        o_sb = sb("o_sb", [P, 2, F], fp32)

        tp = [ctx.enter_context(nc.psum_tensor(f"tp{r}", [P, CC], fp32)) for r in range(RC)]
        acc = [ctx.enter_context(nc.psum_tensor(f"acc{r}", [P, BANK], fp32)) for r in range(2)]

        w_in = sem("w_in")
        a_in = sem("a_in")
        x_in = [sem(f"x_in{g}") for g in range(NG)]
        consts = sem("consts")
        const_step = sem("const_step")
        wT_ready = sem("wT_ready")
        wT_copied = sem("wT_copied")
        a2_ready = sem("a2_ready")
        w2_ready = sem("w2_ready")
        w2_copied = sem("w2_copied")
        xT_ready = sem("xT_ready")
        xT_even = sem("xT_even")
        xT_odd = sem("xT_odd")
        s_copied = sem("s_copied")
        drow_ready = sem("drow_ready")
        drow_copied = sem("drow_copied")
        mag_step = sem("mag_step")
        mag_ready = sem("mag_ready")
        top_ready = sem("top_ready")
        sigma_ready = sem("sigma_ready")
        h_ready = sem("h_ready")
        hhi_done = sem("hhi_done")
        hlo_done = sem("hlo_done")
        adj_in = [sem(f"adj_in{r}") for r in range(2 * NH)]
        u_done = sem("u_done")
        relu_done = sem("relu_done")
        v_done = sem("v_done")
        negmax_done = sem("negmax_done")
        exp_done = sem("exp_done")
        tp_done = sem("tp_done")
        hi_done = sem("hi_done")
        lo_done = sem("lo_done")
        prod_done = sem("prod_done")
        dsum_done = sem("dsum_done")
        rden_done = sem("rden_done")
        scaled_done = sem("scaled_done")
        sum_done = sem("sum_done")
        nmean_done = sem("nmean_done")
        square_done = sem("square_done")
        y_done = sem("y_done")
        veps_done = sem("veps_done")
        rstd_done = sem("rstd_done")
        norm_done = sem("norm_done")
        stored = [sem(f"stored{r}") for r in range(2)]

        block = ctx.enter_context(nc.Block())

        @block.sync
        def _(sp):
            sp.dma_start(w_sb[:], W.rearrange("(b p) k -> p b k", p=P)).then_inc(w_in, 16)
            with nc.allow_non_contiguous_dma(reason="2 x 256 numbers"):
                sp.dma_start(a12[:, :, 0], a1.rearrange("(b p) -> p b", p=P)).then_inc(a_in, 16)
                sp.dma_start(a12[:, :, 1], a2.rearrange("(b p) -> p b", p=P)).then_inc(a_in, 16)
            for g in range(NG):
                ts = slice(g * HG, (g + 1) * HG)
                sp.dma_start(x_sb[:, ts, :], x_v[:, ts, :]).then_inc(x_in[g], 16)

            def load(i, c, ring_used=True):
                for h in range(NH):
                    if ring_used:
                        sp.wait_ge(v_done, NH * PERIOD * i + NH * (c - 2) + h + 1)
                    r = NH * (c % 2) + h
                    sp.dma_start(adj_sb[:, r, :], adj_v[PERIOD * i + c, :, h, :]).then_inc(adj_in[r], 16)

            def store(i, c):
                sp.wait_ge(norm_done, PERIOD * i + c + 1)
                sp.dma_start(out_v[PERIOD * i + c, :, :], o_sb[:, c % 2, :]).then_inc(stored[c % 2], 16)

            LAG = 6
            for t in range(LAG):
                load(0, t, t >= 2)
            with sp.Fori(0, LOOPS) as i:
                for c in range(PERIOD):
                    load(i, c + LAG)
                    store(i, c)
            for t in range(PERIOD * LOOPS, NT):
                if t + LAG < NT:
                    load(0, t + LAG)
                store(0, t)
            for r in range(2):
                sp.wait_ge(stored[r], 16 * (NT // 2))

        @block.gpsimd
        def _(pool):
            nc.gpsimd.memset(ident[:], 0.0).then_inc(const_step, 1)
            pool.wait_ge(const_step, 1)
            nc.gpsimd.affine_select(out=ident[:], in_=ident[:], compare_op=ALU.not_equal, fill=1.0, base=0,
                                    pattern=[[-1, P]], channel_multiplier=1).then_inc(consts, 1)
            nc.gpsimd.memset(powers[:, 0:1], -1.0).then_inc(consts, 1)
            nc.gpsimd.memset(powers[:, 1:2], -0.5).then_inc(consts, 1)
            pool.wait_ge(mag_ready, 1)
            nc.gpsimd.partition_all_reduce(top2[:], mag2[:], P, bass.bass_isa.ReduceOp.max).then_inc(top_ready, 1)

            def inv_sum(i, c, ring_used=True):
                r = c % 2
                pool.wait_ge(exp_done, NH * PERIOD * i + NH * (c + 1))
                if ring_used:
                    pool.wait_ge(scaled_done, PERIOD * i + c - 1)
                nc.gpsimd.nop(nofuse=True)
                nc.gpsimd.tensor_scalar(dsum[:, r:r + 1], den[:, c % 3, 0:1], den[:, c % 3, 1:2], sigma[:, 0:1],
                                        ALU.add, ALU.mult).then_inc(dsum_done, 1)
                pool.wait_ge(dsum_done, PERIOD * i + c + 1)
                nc.gpsimd.tensor_tensor(rden[:, r:r + 1], dsum[:, r:r + 1], powers[:, 0:1],
                                        ALU.pow).then_inc(rden_done, 1)

            def add_x(i, c):
                r = c % 2
                pool.wait_ge(scaled_done, PERIOD * i + c + 1)
                nc.gpsimd.nop(nofuse=True)
                nc.gpsimd.tensor_tensor(y[:, r, :], y[:, r, :],
                                        x_sb[:, bass.ds(PERIOD * i + c, 1), :].rearrange("p t f -> p (t f)"),
                                        ALU.add).then_inc(y_done, 1)

            def minus_mean(i, c):
                r = c % 2
                pool.wait_ge(sum_done, PERIOD * i + c + 1)
                nc.gpsimd.nop(nofuse=True)
                nc.gpsimd.tensor_scalar(nmean[:, r:r + 1], ysum[:, r:r + 1], -1.0 / F, 0.0,
                                        ALU.mult, ALU.add).then_inc(nmean_done, 1)

            def normalise(i, c, ring_used=True):
                r = c % 2
                pool.wait_ge(square_done, PERIOD * i + c + 1)
                nc.gpsimd.nop(nofuse=True)
                nc.gpsimd.tensor_scalar(veps[:, r:r + 1], ysq[:, r:r + 1], 1.0 / F, EPS,
                                        ALU.mult, ALU.add).then_inc(veps_done, 1)
                pool.wait_ge(veps_done, PERIOD * i + c + 1)
                nc.gpsimd.tensor_tensor(rstd[:, r:r + 1], veps[:, r:r + 1], powers[:, 1:2],
                                        ALU.pow).then_inc(rstd_done, 1)
                pool.wait_ge(rstd_done, PERIOD * i + c + 1)
                if ring_used:
                    pool.wait_ge(stored[r], 16 * (PERIOD // 2) * i + 16 * (c // 2))
                nc.gpsimd.nop(nofuse=True)
                nc.gpsimd.tensor_scalar(o_sb[:, r, :], y[:, r, :], nmean[:, r:r + 1], rstd[:, r:r + 1],
                                        ALU.add, ALU.mult).then_inc(norm_done, 1)

            def tile(i, c):
                t = c if type(i) is int else None
                if t is None or t >= 2:
                    normalise(i, c - 2, t is None or t >= 4)
                if t is None or t < NT:
                    inv_sum(i, c, t is None or t >= 2)
                if t is None or 1 <= t <= NT:
                    add_x(i, c - 1)
                    minus_mean(i, c - 1)

            for t in range(4):
                tile(0, t)
            with pool.Fori(0, LOOPS) as i:
                for c in range(4, PERIOD + 4):
                    tile(i, c)
            for t in range(LOOPS * PERIOD + 4, NT + 2):
                tile(0, t)

        @block.scalar
        def _(act):
            def d_group(g):
                act.wait_ge(drow_ready, g + 1)
                nc.scalar.activation(d_row[:, g * GC:(g + 1) * GC], acc[g % 2][:, 0:GC], ACT.Copy,
                                     scale=(1 - ALPHA) / BIG).then_inc(drow_copied, 1)

            for g in range(NG):
                if g % 2:
                    act.wait_ge(xT_ready, g + 1)
                    nc.scalar.copy(xT[:, :, g * GC:(g + 1) * GC],
                                   tp[g % RC][:].rearrange("p (b n) -> p b n", b=KB)).then_inc(xT_odd, 1)
                if g >= 1:
                    d_group(g - 1)
            d_group(NG - 1)

            def relu(i, c, h, ring_used=True):
                if ring_used:
                    act.wait_ge(tp_done, NC * PERIOD * i + NC * (c - 2) + 2 * h + 2)
                    nc.scalar.nop(nofuse=True)
                nc.scalar.activation(w[:, c % 2, h * HC:(h + 1) * HC], d_row[:, h * HC:(h + 1) * HC], ACT.Relu,
                                     bias=s_col[:, bass.ds(PERIOD * i + c, 1)], scale=R).then_inc(relu_done, 1)

            def expo(i, c, h, ring_used=True):
                if h == 0:
                    act.wait_ge(negmax_done, PERIOD * i + c + 1)
                    if ring_used:
                        act.wait_ge(dsum_done, PERIOD * i + c - 2)
                v = w[:, c % 2, h * HC:(h + 1) * HC]
                nc.scalar.activation(v, v, ACT.Exp, bias=negmax[:, c % 2:c % 2 + 1], scale=BIG / R,
                                     accum_out=den[:, c % 3, h:h + 1]).then_inc(exp_done, 1)

            def high(i, c, k, ring_used=True):
                act.wait_ge(tp_done, NC * PERIOD * i + NC * c + k + 1)
                if ring_used:
                    act.wait_ge(prod_done, NC * PERIOD * i + NC * c + k - RC + 1)
                r = (NC * c + k + NP) % RC
                nc.scalar.copy(e_hi[:, r, :], tp[r][:]).then_inc(hi_done, 1)

            def scaled(i, c, ring_used=True):
                r = c % 2
                act.wait_ge(prod_done, NC * PERIOD * i + NC * (c + 1))
                act.wait_ge(rden_done, PERIOD * i + c + 1)
                if ring_used:
                    act.wait_ge(norm_done, PERIOD * i + c - 1)
                nc.scalar.activation(y[:, r, :], acc[r][:, 0:F], ACT.Copy, scale=rden[:, r:r + 1]
                                     ).then_inc(scaled_done, 1)

            def sum_y(i, c):
                r = c % 2
                act.wait_ge(y_done, PERIOD * i + c + 1)
                nc.scalar.activation(unused[:, 0, :], y[:, r, :], ACT.Copy,
                                     accum_out=ysum[:, r:r + 1]).then_inc(sum_done, 1)

            def square_y(i, c):
                r = c % 2
                act.wait_ge(nmean_done, PERIOD * i + c + 1)
                nc.scalar.activation(unused[:, 1, :], y[:, r, :], ACT.Square, bias=nmean[:, r:r + 1],
                                     accum_out=ysq[:, r:r + 1]).then_inc(square_done, 1)

            act.wait_ge(drow_copied, NG)
            act.wait_ge(sigma_ready, 1)
            for g in range(NP):
                act.wait_ge(h_ready, g + 1)
                hp = tp[g % RC][:].rearrange("p (t f) -> p t f", t=TP)[:, :, 0:F]
                nc.scalar.activation(h_hi[:, g * TP:(g + 1) * TP, :], hp, ACT.Copy, scale=sigma[:, 0:1]
                                     ).then_inc(hhi_done, 1)
                if g == 0:
                    act.wait_ge(s_copied, 1)
                if g < 4:
                    relu(0, g // 2, g % 2, False)
                if g == 8:
                    expo(0, 0, 0, False)
                if g == 10:
                    expo(0, 0, 1, False)

            def tile(i, c):
                t = c if type(i) is int else None
                high(i, c, 0, t != 0)
                if t is None or t + 2 < NT:
                    relu(i, c + 2, 0)
                if t is None or t >= 2:
                    square_y(i, c - 2)
                high(i, c, 1, t != 0)
                if t is None or t + 1 < NT:
                    expo(i, c + 1, 0, t is None or t >= 2)
                if t != 0:
                    scaled(i, c - 1, t is None or t >= 3)
                high(i, c, 2, t != 0)
                if t is None or t + 1 < NT:
                    expo(i, c + 1, 1)
                high(i, c, 3)
                if t is None or t + 2 < NT:
                    relu(i, c + 2, 1)
                if t != 0:
                    sum_y(i, c - 1)

            tile(0, 0)
            tile(0, 1)
            for t in range(2, PERIOD + 1):
                tile(0, t)
            with act.Fori(1, LOOPS) as i:
                for c in range(1, PERIOD + 1):
                    tile(i, c)
            for t in PEELED:
                tile(0, t)
            square_y(0, NT - 2)
            scaled(0, NT - 1)
            sum_y(0, NT - 1)
            square_y(0, NT - 1)

        @block.vector
        def _(dve):
            def magnitude(g):
                dve.wait_ge(x_in[g], 16)
                nc.vector.tensor_reduce(mags[:, g:g + 1], x_sb[:, g * HG:(g + 1) * HG, :], AX.XY, ALU.max,
                                        apply_absolute_value=True).then_inc(mag_step, 1)

            dve.wait_ge(a_in, 32)
            nc.vector.tensor_copy(a2_rep[:], a12[:, :, 1:2].broadcast_to([P, KB, P])).then_inc(a2_ready, 1)
            dve.wait_ge(wT_ready, 1)
            nc.vector.tensor_copy(wT[:, :, 0:F], tp[0][:, 0:KB * F].rearrange("p (b f) -> p b f", b=KB)
                                  ).then_inc(wT_copied, 1)
            nc.vector.tensor_copy(wT[:, :, F], tp[1][:, 0:KB]).then_inc(wT_copied, 1)
            dve.wait_ge(w2_ready, 1)
            nc.vector.tensor_copy(w2_rep[:], tp[1][:, BANK:BANK + KB * P].rearrange("p (b m) -> p b m", b=KB)
                                  ).then_inc(w2_copied, 1)
            for g in range(NG):
                if g % 2 == 0:
                    dve.wait_ge(xT_ready, g + 1)
                    nc.vector.tensor_copy(xT[:, :, g * GC:(g + 1) * GC],
                                          tp[g % RC][:].rearrange("p (b n) -> p b n", b=KB)
                                          ).then_inc(xT_even, 1)
                magnitude(g)

            nc.vector.tensor_reduce(mag2[:, 1:2], w_sb[:], AX.XY, ALU.max,
                                    apply_absolute_value=True).then_inc(mag_step, 1)
            dve.wait_ge(mag_step, NG + 1)
            nc.vector.tensor_reduce(mag2[:, 0:1], mags[:, 0:NG], AX.X, ALU.max).then_inc(mag_ready, 1)
            dve.wait_ge(top_ready, 1)
            nc.vector.tensor_scalar(bound[:], top2[:, 0:1], top2[:, 1:2], float(F), ALU.mult, ALU.mult
                                    ).then_inc(mag_step, 1)
            dve.wait_ge(mag_step, NG + 2)
            nc.vector.tensor_scalar(rpow2[:], bound[:], 1e-30, None, ALU.max).then_inc(mag_step, 1)
            dve.wait_ge(mag_step, NG + 3)
            nc.vector.tensor_scalar(pow2[:].bitcast(i32), rpow2[:].bitcast(i32), 0x7F800000, None,
                                    ALU.bitwise_and).then_inc(mag_step, 1)
            dve.wait_ge(mag_step, NG + 4)
            nc.vector.reciprocal(rpow2[:], pow2[:]).then_inc(mag_step, 1)
            dve.wait_ge(mag_step, NG + 5)
            nc.vector.tensor_scalar(sigma[:], rpow2[:], HTOP, None, ALU.mult).then_inc(sigma_ready, 1)

            def edges(i, c, h):
                r = NH * (c % 2) + h
                dve.wait_ge(adj_in[r], 16 * (PERIOD // 2) * i + 16 * (c // 2 + 1))
                nc.vector.scalar_tensor_tensor(
                    out=adj_sb[:, r, :].bitcast(fp32), in0=adj_sb[:, r, :], scalar=0.0,
                    in1=d_row[:, h * HC:(h + 1) * HC], op0=ALU.is_equal, op1=ALU.subtract).then_inc(u_done, 1)

            def scores(i, c, h):
                r = NH * (c % 2) + h
                dve.wait_ge(u_done, NH * PERIOD * i + NH * c + h + 1)
                dve.wait_ge(relu_done, NH * PERIOD * i + NH * c + h + 1)
                if h:
                    dve.wait_ge(v_done, NH * PERIOD * i + NH * c + h)
                nc.vector.nop(nofuse=True)
                v = w[:, c % 2, h * HC:(h + 1) * HC]
                nc.vector.tensor_tensor_reduce(
                    out=v, in0=v, in1=adj_sb[:, r, :].bitcast(fp32), scale=1.0,
                    scalar=(wmax[:, c % 2, h - 1:h] if h else -3e38), op0=ALU.subtract, op1=ALU.max,
                    accum_out=wmax[:, c % 2, h:h + 1]).then_inc(v_done, 1)

            def row_max(i, c, ring_used=True):
                dve.wait_ge(v_done, NH * PERIOD * i + NH * (c + 1))
                if ring_used:
                    dve.wait_ge(exp_done, NH * PERIOD * i + NH * (c - 1))
                nc.vector.tensor_scalar(negmax[:, c % 2:c % 2 + 1], wmax[:, c % 2, NH - 1:NH], -BIG / R, SHIFT,
                                        ALU.mult, ALU.add).then_inc(negmax_done, 1)

            def low(i, c, k):
                dve.wait_ge(hi_done, NC * PERIOD * i + NC * c + k + 1)
                r = (NC * c + k + NP) % RC
                nc.vector.tensor_tensor(e_lo[:, r, :], tp[r][:], e_hi[:, r, :], ALU.subtract
                                        ).then_inc(lo_done, 1)

            dve.wait_ge(drow_copied, NG)
            for g in range(NP):
                dve.wait_ge(hhi_done, g + 1)
                hs = tp[g % RC][:].rearrange("p (t f) -> p t f", t=TP)
                nc.vector.tensor_scalar(s_col[:, g * TP:(g + 1) * TP], hs[:, :, F], R * (1 - ALPHA) / BIG, None,
                                        ALU.mult).then_inc(s_copied, 1)
                nc.vector.scalar_tensor_tensor(
                    out=h_lo[:, g * TP:(g + 1) * TP, :], in0=hs[:, :, 0:F], scalar=sigma[:, 0:1],
                    in1=h_hi[:, g * TP:(g + 1) * TP, :], op0=ALU.mult, op1=ALU.subtract).then_inc(hlo_done, 1)
                if g == 0:
                    edges(0, 0, 0)
                elif g == 2:
                    scores(0, 0, 0)
                elif g == 3:
                    edges(0, 0, 1)
                elif g == 5:
                    scores(0, 0, 1)
                    row_max(0, 0, False)
                elif g == 8:
                    edges(0, 1, 0)
                elif g == 10:
                    scores(0, 1, 0)
                elif g == 12:
                    edges(0, 1, 1)

            def tile(i, c):
                t = c if type(i) is int else None
                low(i, c, 0)
                if t is None or t + 1 < NT:
                    scores(i, c + 1, 1)
                    row_max(i, c + 1, t is None or t >= 1)
                low(i, c, 1)
                if t is None or t + 2 < NT:
                    edges(i, c + 2, 0)
                low(i, c, 2)
                if t is None or t + 2 < NT:
                    scores(i, c + 2, 0)
                low(i, c, 3)
                if t is None or t + 2 < NT:
                    edges(i, c + 2, 1)

            for t in range(PERIOD + 1):
                tile(0, t)
            with dve.Fori(1, LOOPS) as i:
                for c in range(1, PERIOD + 1):
                    tile(i, c)
            for t in PEELED:
                tile(0, t)

        @block.tensor
        def _(pe):
            pe.wait_ge(consts, 1)
            pe.wait_ge(w_in, 16)
            pe.wait_ge(a_in, 32)
            for b in range(KB):
                for fb in range(KB):
                    nc.tensor.matmul(tp[1][:, b:b + 1], w_sb[:, fb, b * P:(b + 1) * P], a12[:, fb, 0:1],
                                     start=(fb == 0), stop=(fb == KB - 1))
            for b in range(KB):
                for fb in range(KB):
                    last = nc.tensor.transpose(tp[0][:, b * F + fb * P:b * F + (fb + 1) * P],
                                               w_sb[:, fb, b * P:(b + 1) * P], ident[:])
            last.then_inc(wT_ready, 1)
            pe.wait_ge(a2_ready, 1)
            for b in range(KB):
                for fb in range(KB):
                    last = nc.tensor.matmul(tp[1][:, BANK + b * P:BANK + (b + 1) * P],
                                            w_sb[:, fb, b * P:(b + 1) * P], a2_rep[:, fb, :],
                                            start=(fb == 0), stop=(fb == KB - 1))
            last.then_inc(w2_ready, 1)

            def d_group(g):
                pe.wait_ge(xT_odd if g % 2 else xT_even, g // 2 + 1)
                if g >= 2:
                    pe.wait_ge(drow_copied, g - 1)
                for b in range(KB):
                    last = nc.tensor.matmul(acc[g % 2][:, 0:GC], w2_rep[:, b, :], xT[:, b, g * GC:(g + 1) * GC],
                                            start=(b == 0), stop=(b == KB - 1))
                last.then_inc(drow_ready, 1)

            for g in range(NG):
                pe.wait_ge(x_in[g], 16)
                if g == 0:
                    pe.wait_ge(wT_copied, 2)
                if g == 1:
                    pe.wait_ge(w2_copied, 1)
                if g >= RC:
                    before = g - RC
                    pe.wait_ge(xT_odd if before % 2 else xT_even, before // 2 + 1)
                for b in range(KB):
                    for u in range(HG):
                        last = nc.tensor.transpose(tp[g % RC][:, (b * HG + u) * P:(b * HG + u + 1) * P],
                                                   x_sb[:, g * HG + u, b * P:(b + 1) * P], ident[:])
                last.then_inc(xT_ready, 1)
                if g >= 1:
                    d_group(g - 1)
            d_group(NG - 1)
            for g in range(NP):
                if g >= RC:
                    pe.wait_ge(hlo_done, g - RC + 1)
                for u in range(TP):
                    t = g * TP + u
                    for b in range(KB):
                        last = nc.tensor.matmul(tp[g % RC][:, u * BANK:u * BANK + F + 1],
                                                xT[:, b, t * P:(t + 1) * P], wT[:, b, :],
                                                start=(b == 0), stop=(b == KB - 1))
                last.then_inc(h_ready, 1)

            def flip(i, c, k, ring_used=True):
                if k % 2 == 0:
                    pe.wait_ge(exp_done, NH * PERIOD * i + NH * c + k // 2 + 1)
                if ring_used:
                    pe.wait_ge(lo_done, NC * PERIOD * i + NC * c + k - RC + 1)
                r = (NC * c + k + NP) % RC
                for b in range(CB):
                    j = k * CB + b
                    last = nc.tensor.transpose(tp[r][:, b * P:(b + 1) * P], w[:, c % 2, j * P:(j + 1) * P], ident[:])
                last.then_inc(tp_done, 1)

            def product(i, c, k, ring_used=True):
                r = (NC * c + k + NP) % RC
                sums = acc[c % 2][:, 0:F]
                if k == 0 and ring_used:
                    pe.wait_ge(scaled_done, PERIOD * i + c - 1)
                pe.wait_ge(lo_done, NC * PERIOD * i + NC * c + k + 1)
                for b in range(CB):
                    j = k * CB + b
                    hi = e_hi[:, r, b * P:(b + 1) * P]
                    nc.tensor.matmul(sums, hi, h_hi[:, j, :], start=(j == 0), stop=False)
                    nc.tensor.matmul(sums, hi, h_lo[:, j, :], start=False, stop=False)
                    last = nc.tensor.matmul(sums, e_lo[:, r, b * P:(b + 1) * P], h_hi[:, j, :],
                                            start=False, stop=(j == NT - 1))
                last.then_inc(prod_done, 1)

            def tile(i, c):
                t = c if type(i) is int else None
                for k in range(NC):
                    if k + 2 < NC:
                        flip(i, c, k + 2, t != 0 or k + 2 >= RC)
                    elif t is None or t + 1 < NT:
                        flip(i, c + 1, k + 2 - NC)
                    product(i, c, k, t is None or t >= 2)

            for k in range(2):
                pe.wait_ge(hlo_done, NP - RC + 1 + k)
                flip(0, 0, k, False)
            pe.wait_ge(hlo_done, NP)
            for t in range(PERIOD + 1):
                tile(0, t)
            with pe.Fori(1, LOOPS) as i:
                for c in range(1, PERIOD + 1):
                    tile(i, c)
            for t in PEELED:
                tile(0, t)


_INS = ['x', 'adj', 'L0_gnn_W', 'L0_gnn_a1', 'L0_gnn_a2']


def kernel(**inputs):
    import numpy as _np
    import concourse.bacc as _bacc
    from concourse import mybir as _mybir
    from concourse.bass_utils import run_bass_kernel_spmd as _run

    nc = _bacc.Bacc("TRN2", target_bir_lowering=False, num_devices=1)
    arrays, args = {}, []
    for name in _INS:
        a = _np.ascontiguousarray(inputs[name])
        arrays[f"in_{name}_dram"] = a
        args.append(nc.dram_tensor(f"in_{name}_dram", a.shape, _mybir.dt.from_np(a.dtype), kind="ExternalInput").ap())
    shape = inputs['x'].shape
    out = nc.dram_tensor("out_0_dram", shape, _mybir.dt.float32, kind="ExternalOutput").ap()
    gat_layer(nc, *args, out)
    r = _run(nc, [arrays], core_ids=[0])
    return r.results[0]["out_0_dram"]
```

```python
import concourse.bass as bass
from concourse import mybir
from contextlib import ExitStack


fp32 = mybir.dt.float32
fp16 = mybir.dt.float16
i32 = mybir.dt.int32
ALU = mybir.AluOpType
ACT = mybir.ActivationFunctionType
AX = mybir.AxisListType

P = 128
ALPHA = 0.2
R = 4.0
BIG = 2.0 ** 62
SHIFT = 10.0
EPS = 1e-5
HTOP = 2.0 ** 14
BANK = 512
PERIOD = 6


def gat_layer(nc, x, adj, W, a1, a2, identity, out):
    N, F = x.shape
    NT = N // P
    KB = F // P
    NH = 2
    HC = N // NH
    NC = 4
    CC = N // NC
    CB = CC // P
    RC = 3
    HG = CC // F
    NG = NT // HG
    GC = HG * P
    TP = 2
    NP = NT // TP
    LOOPS = (NT - 3) // PERIOD
    PEELED = range(LOOPS * PERIOD + 1, NT)

    adj_v = adj.rearrange("(t p) (h c) -> t p h c", p=P, h=NH)
    x_v = x.rearrange("(t p) f -> p t f", p=P)
    out_v = out.rearrange("(t p) f -> t p f", p=P)

    ctx = ExitStack()
    with ctx:
        def sb(name, shape, dt):
            return ctx.enter_context(nc.sbuf_tensor(name, shape, dt))

        def sem(name):
            return ctx.enter_context(nc.semaphore(name))

        x_sb = sb("x_sb", [P, NT, F], fp32)
        h_hi = sb("h_hi", [P, NT, F], fp16)
        h_lo = sb("h_lo", [P, NT, F], fp16)
        d_row = sb("d_row", [P, N], fp32)
        s_col = sb("s_col", [P, NT], fp32)
        ident = sb("ident", [P, P], fp32)
        powers = sb("powers", [P, 3], fp32)
        w_sb = sb("w_sb", [P, KB, F], fp32)
        wT = sb("wT", [P, KB, F + 1], fp32)
        a12 = sb("a12", [P, KB, 2], fp32)
        a2_rep = sb("a2_rep", [P, KB, P], fp32)
        w2_row = sb("w2_row", [P, F], fp32)
        d_col = sb("d_col", [P, NT], fp32)
        xT = sb("xT", [P, KB, N], fp32)
        xsq = sb("xsq", [P, NG], fp32)
        xsq_max = sb("xsq_max", [P, 1], fp32)
        mag2 = sb("mag2", [P, 2], fp32)
        top2 = sb("top2", [1, 2], fp32)
        bound = sb("bound", [1, 1], fp32)
        pow2 = sb("pow2", [1, 1], fp32)
        rpow2 = sb("rpow2", [1, 1], fp32)
        sigma1 = sb("sigma1", [1, 1], fp32)
        ones = sb("ones", [1, P], fp32)
        sigma = sb("sigma", [P, 1], fp32)
        adj_sb = sb("adj_sb", [P, 2 * NH, HC], i32)
        w = sb("w", [P, 2, N], fp32)
        half_ring = RC * CC // 2
        e_hi = xT[:, 0, 0:half_ring].bitcast(fp16).rearrange("p (r c) -> p r c", r=RC)
        e_lo = xT[:, 1, 0:half_ring].bitcast(fp16).rearrange("p (r c) -> p r c", r=RC)
        d_terms = w[:, 1, :].rearrange("p (t f) -> p t f", f=F)
        sq_act = h_lo[:].rearrange("p t f -> p (t f)").bitcast(fp32).rearrange("p (g t f) -> p g t f", t=HG, f=F)
        sq_dve = w[:, 0, :].rearrange("p (g t f) -> p g t f", t=HG, f=F)
        wmax = sb("wmax", [P, 2, NH], fp32)
        negmax = sb("negmax", [P, 2], fp32)
        den = sb("den", [P, 3, NH], fp32)
        dsum = sb("dsum", [P, 2], fp32)
        rden = sb("rden", [P, 2], fp32)
        y = sb("y", [P, 2, F], fp32)
        ysum = sb("ysum", [P, 2], fp32)
        nmean = sb("nmean", [P, 2], fp32)
        ysq = sb("ysq", [P, 2], fp32)
        unused = sb("unused", [P, 2, F], fp32)
        veps = sb("veps", [P, 2], fp32)
        rstd = sb("rstd", [P, 2], fp32)
        o_sb = sb("o_sb", [P, 2, F], fp32)

        tp = [ctx.enter_context(nc.psum_tensor(f"tp{r}", [P, CC], fp32)) for r in range(RC)]
        acc = [ctx.enter_context(nc.psum_tensor(f"acc{r}", [P, BANK], fp32)) for r in range(2)]

        w_in = sem("w_in")
        a1_in = sem("a1_in")
        a2_in = sem("a2_in")
        x_in = [sem(f"x_in{g}") for g in range(NG)]
        ident_in = sem("ident_in")
        consts = sem("consts")
        a2_ready = sem("a2_ready")
        w2_ready = sem("w2_ready")
        w2_copied = sem("w2_copied")
        wT_ready = sem("wT_ready")
        wT_copied = sem("wT_copied")
        xT_ready = sem("xT_ready")
        xT_copied = sem("xT_copied")
        dcol_done = sem("dcol_done")
        drow_ready = sem("drow_ready")
        drow_copied = sem("drow_copied")
        xsq_act_done = sem("xsq_act_done")
        xsq_dve_done = sem("xsq_dve_done")
        xsq_read = sem("xsq_read")
        xroot_ready = sem("xroot_ready")
        wmax_ready = sem("wmax_ready")
        magT_ready = sem("magT_ready")
        top_step = sem("top_step")
        sigma1_ready = sem("sigma1_ready")
        sigma_spread = sem("sigma_spread")
        sigma_ready = sem("sigma_ready")
        h_ready = sem("h_ready")
        s_copied = sem("s_copied")
        hhi_done = sem("hhi_done")
        hlo_done = sem("hlo_done")
        adj_in = [sem(f"adj_in{r}") for r in range(2 * NH)]
        u_done = sem("u_done")
        relu_done = sem("relu_done")
        v_done = sem("v_done")
        negmax_done = sem("negmax_done")
        exp_done = sem("exp_done")
        tp_done = sem("tp_done")
        hi_done = sem("hi_done")
        lo_done = sem("lo_done")
        prod_done = sem("prod_done")
        dsum_done = sem("dsum_done")
        rden_done = sem("rden_done")
        scaled_done = sem("scaled_done")
        sum_done = sem("sum_done")
        nmean_done = sem("nmean_done")
        square_done = sem("square_done")
        y_done = sem("y_done")
        veps_done = sem("veps_done")
        rstd_done = sem("rstd_done")
        norm_done = sem("norm_done")
        stored = [sem(f"stored{r}") for r in range(2)]

        block = ctx.enter_context(nc.Block())

        @block.sync
        def _(sp):
            sp.dma_start(w_sb[:], W.rearrange("(b p) k -> p b k", p=P)).then_inc(w_in, 16)
            for g in range(NG):
                ts = slice(g * HG, (g + 1) * HG)
                sp.dma_start(x_sb[:, ts, :], x_v[:, ts, :]).then_inc(x_in[g], 16)

            def load(i, c, ring_used=True):
                for h in range(NH):
                    if ring_used:
                        sp.wait_ge(v_done, NH * PERIOD * i + NH * (c - 2) + h + 1)
                    r = NH * (c % 2) + h
                    sp.dma_start(adj_sb[:, r, :], adj_v[PERIOD * i + c, :, h, :]).then_inc(adj_in[r], 16)

            def store(i, c):
                sp.wait_ge(norm_done, PERIOD * i + c + 1)
                sp.dma_start(out_v[PERIOD * i + c, :, :], o_sb[:, c % 2, :]).then_inc(stored[c % 2], 16)

            LAG = 6
            for t in range(LAG):
                load(0, t, t >= 2)
            with sp.Fori(0, LOOPS) as i:
                for c in range(PERIOD):
                    load(i, c + LAG)
                    store(i, c)
            for t in range(PERIOD * LOOPS, NT):
                if t + LAG < NT:
                    load(0, t + LAG)
                store(0, t)
            for r in range(2):
                sp.wait_ge(stored[r], 16 * (NT // 2))

        @block.gpsimd
        def _(pool):
            nc.gpsimd.memset(ones[:], 1.0).then_inc(consts, 1)
            nc.gpsimd.memset(powers[:, 0:1], -1.0).then_inc(consts, 1)
            nc.gpsimd.memset(powers[:, 1:2], -0.5).then_inc(consts, 1)
            nc.gpsimd.memset(powers[:, 2:3], 0.5).then_inc(consts, 1)
            pool.wait_ge(consts, 4)
            pool.wait_ge(xsq_read, 1)
            nc.gpsimd.tensor_tensor(mag2[:, 0:1], xsq_max[:], powers[:, 2:3], ALU.pow).then_inc(xroot_ready, 1)

            def inv_sum(i, c, ring_used=True):
                r = c % 2
                pool.wait_ge(exp_done, NH * PERIOD * i + NH * (c + 1))
                if ring_used:
                    pool.wait_ge(scaled_done, PERIOD * i + c - 1)
                nc.gpsimd.nop(nofuse=True)
                nc.gpsimd.tensor_scalar(dsum[:, r:r + 1], den[:, c % 3, 0:1], den[:, c % 3, 1:2], sigma[:, 0:1],
                                        ALU.add, ALU.mult).then_inc(dsum_done, 1)
                pool.wait_ge(dsum_done, PERIOD * i + c + 1)
                nc.gpsimd.tensor_tensor(rden[:, r:r + 1], dsum[:, r:r + 1], powers[:, 0:1],
                                        ALU.pow).then_inc(rden_done, 1)

            def add_x(i, c):
                r = c % 2
                pool.wait_ge(scaled_done, PERIOD * i + c + 1)
                nc.gpsimd.nop(nofuse=True)
                nc.gpsimd.tensor_tensor(y[:, r, :], y[:, r, :],
                                        x_sb[:, bass.ds(PERIOD * i + c, 1), :].rearrange("p t f -> p (t f)"),
                                        ALU.add).then_inc(y_done, 1)

            def minus_mean(i, c):
                r = c % 2
                pool.wait_ge(sum_done, PERIOD * i + c + 1)
                nc.gpsimd.nop(nofuse=True)
                nc.gpsimd.tensor_scalar(nmean[:, r:r + 1], ysum[:, r:r + 1], -1.0 / F, 0.0,
                                        ALU.mult, ALU.add).then_inc(nmean_done, 1)

            def normalise(i, c, ring_used=True):
                r = c % 2
                pool.wait_ge(square_done, PERIOD * i + c + 1)
                nc.gpsimd.nop(nofuse=True)
                nc.gpsimd.tensor_scalar(veps[:, r:r + 1], ysq[:, r:r + 1], 1.0 / F, EPS,
                                        ALU.mult, ALU.add).then_inc(veps_done, 1)
                pool.wait_ge(veps_done, PERIOD * i + c + 1)
                nc.gpsimd.tensor_tensor(rstd[:, r:r + 1], veps[:, r:r + 1], powers[:, 1:2],
                                        ALU.pow).then_inc(rstd_done, 1)
                pool.wait_ge(rstd_done, PERIOD * i + c + 1)
                if ring_used:
                    pool.wait_ge(stored[r], 16 * (PERIOD // 2) * i + 16 * (c // 2))
                nc.gpsimd.nop(nofuse=True)
                nc.gpsimd.tensor_scalar(o_sb[:, r, :], y[:, r, :], nmean[:, r:r + 1], rstd[:, r:r + 1],
                                        ALU.add, ALU.mult).then_inc(norm_done, 1)

            def tile(i, c):
                t = c if type(i) is int else None
                if t is None or t >= 2:
                    normalise(i, c - 2, t is None or t >= 4)
                if t is None or t < NT:
                    inv_sum(i, c, t is None or t >= 2)
                if t is None or 1 <= t <= NT:
                    add_x(i, c - 1)
                    minus_mean(i, c - 1)

            for t in range(4):
                tile(0, t)
            with pool.Fori(0, LOOPS) as i:
                for c in range(4, PERIOD + 4):
                    tile(i, c)
            for t in range(LOOPS * PERIOD + 4, NT + 2):
                tile(0, t)

        @block.scalar
        def _(act):
            with nc.allow_non_contiguous_dma(reason="2 x 256 numbers"):
                act.dma_start(a12[:, :, 1], a2.rearrange("(b p) -> p b", p=P)).then_inc(a2_in, 16)
                act.dma_start(a12[:, :, 0], a1.rearrange("(b p) -> p b", p=P)).then_inc(a1_in, 16)
            act.dma_start(ident[:], identity).then_inc(ident_in, 16)

            def d_row_group(g):
                act.wait_ge(drow_ready, g + 1)
                nc.scalar.activation(d_row[:, g * GC:(g + 1) * GC], acc[g % 2][:, 0:GC], ACT.Copy,
                                     scale=(1 - ALPHA) / BIG).then_inc(drow_copied, 1)

            act.wait_ge(wT_ready, 1)
            nc.scalar.copy(wT[:, :, 0:F], acc[1][:, 0:KB * F].rearrange("p (b f) -> p b f", b=KB)
                           ).then_inc(wT_copied, 1)
            nc.scalar.copy(wT[:, :, F], tp[2][:, 0:KB]).then_inc(wT_copied, 1)
            for g in range(NG):
                act.wait_ge(xT_ready, g + 1)
                nc.scalar.copy(xT[:, :, g * GC:(g + 1) * GC],
                               tp[g % RC][:].rearrange("p (b n) -> p b n", b=KB)).then_inc(xT_copied, 1)
                if g < NG // 2:
                    nc.scalar.activation(sq_act[:, g], x_sb[:, g * HG:(g + 1) * HG, :], ACT.Square,
                                         accum_out=xsq[:, g:g + 1]).then_inc(xsq_act_done, 1)
                if g >= 2:
                    d_row_group(g - 2)
            d_row_group(NG - 2)
            d_row_group(NG - 1)

            def relu(i, c, h, ring_used=True):
                if ring_used:
                    act.wait_ge(tp_done, NC * PERIOD * i + NC * (c - 2) + 2 * h + 2)
                    nc.scalar.nop(nofuse=True)
                nc.scalar.activation(w[:, c % 2, h * HC:(h + 1) * HC], d_row[:, h * HC:(h + 1) * HC], ACT.Relu,
                                     bias=s_col[:, bass.ds(PERIOD * i + c, 1)], scale=R).then_inc(relu_done, 1)

            def expo(i, c, h, ring_used=True):
                if h == 0:
                    act.wait_ge(negmax_done, PERIOD * i + c + 1)
                    if ring_used:
                        act.wait_ge(dsum_done, PERIOD * i + c - 2)
                v = w[:, c % 2, h * HC:(h + 1) * HC]
                nc.scalar.activation(v, v, ACT.Exp, bias=negmax[:, c % 2:c % 2 + 1], scale=BIG / R,
                                     accum_out=den[:, c % 3, h:h + 1]).then_inc(exp_done, 1)

            def high(i, c, k, ring_used=True):
                act.wait_ge(tp_done, NC * PERIOD * i + NC * c + k + 1)
                if ring_used:
                    act.wait_ge(prod_done, NC * PERIOD * i + NC * c + k - RC + 1)
                r = (NC * c + k + NP) % RC
                nc.scalar.copy(e_hi[:, r, :], tp[r][:]).then_inc(hi_done, 1)

            def scaled(i, c, ring_used=True):
                r = c % 2
                act.wait_ge(prod_done, NC * PERIOD * i + NC * (c + 1))
                act.wait_ge(rden_done, PERIOD * i + c + 1)
                if ring_used:
                    act.wait_ge(norm_done, PERIOD * i + c - 1)
                nc.scalar.activation(y[:, r, :], acc[r][:, 0:F], ACT.Copy, scale=rden[:, r:r + 1]
                                     ).then_inc(scaled_done, 1)

            def sum_y(i, c):
                r = c % 2
                act.wait_ge(y_done, PERIOD * i + c + 1)
                nc.scalar.activation(unused[:, 0, :], y[:, r, :], ACT.Copy,
                                     accum_out=ysum[:, r:r + 1]).then_inc(sum_done, 1)

            def square_y(i, c):
                r = c % 2
                act.wait_ge(nmean_done, PERIOD * i + c + 1)
                nc.scalar.activation(unused[:, 1, :], y[:, r, :], ACT.Square, bias=nmean[:, r:r + 1],
                                     accum_out=ysq[:, r:r + 1]).then_inc(square_done, 1)

            act.wait_ge(drow_copied, NG)
            act.wait_ge(s_copied, 1)
            act.wait_ge(xsq_read, 1)
            relu(0, 0, 0, False)
            act.wait_ge(sigma_ready, 1)
            for g in range(NP):
                act.wait_ge(h_ready, g + 1)
                hp = tp[g % RC][:].rearrange("p (t f) -> p t f", t=TP)[:, :, 0:F]
                nc.scalar.activation(h_hi[:, g * TP:(g + 1) * TP, :], hp, ACT.Copy, scale=sigma[:, 0:1]
                                     ).then_inc(hhi_done, 1)
                if g in (1, 3, 5):
                    relu(0, (g + 1) // 4, (g + 1) // 2 % 2, False)
                if g == 8:
                    expo(0, 0, 0, False)
                if g == 12:
                    expo(0, 0, 1, False)

            def tile(i, c):
                t = c if type(i) is int else None
                high(i, c, 0, t != 0)
                if t is None or t + 2 < NT:
                    relu(i, c + 2, 0)
                if t is None or t >= 2:
                    square_y(i, c - 2)
                high(i, c, 1, t != 0)
                if t is None or t + 1 < NT:
                    expo(i, c + 1, 0, t is None or t >= 2)
                if t != 0:
                    scaled(i, c - 1, t is None or t >= 3)
                high(i, c, 2, t != 0)
                if t is None or t + 1 < NT:
                    expo(i, c + 1, 1)
                high(i, c, 3)
                if t is None or t + 2 < NT:
                    relu(i, c + 2, 1)
                if t != 0:
                    sum_y(i, c - 1)

            tile(0, 0)
            tile(0, 1)
            for t in range(2, PERIOD + 1):
                tile(0, t)
            with act.Fori(1, LOOPS) as i:
                for c in range(1, PERIOD + 1):
                    tile(i, c)
            for t in PEELED:
                tile(0, t)
            square_y(0, NT - 2)
            scaled(0, NT - 1)
            sum_y(0, NT - 1)
            square_y(0, NT - 1)

        @block.vector
        def _(dve):
            dve.wait_ge(a2_in, 16)
            nc.vector.tensor_copy(a2_rep[:], a12[:, :, 1:2].broadcast_to([P, KB, P])).then_inc(a2_ready, 1)
            dve.wait_ge(w_in, 16)
            nc.vector.tensor_reduce(mag2[:, 1:2], w_sb[:], AX.XY, ALU.max,
                                    apply_absolute_value=True).then_inc(wmax_ready, 1)
            dve.wait_ge(w2_ready, 1)
            nc.vector.tensor_copy(w2_row[:], acc[0][:, 0:F]).then_inc(w2_copied, 1)
            dve.wait_ge(w2_copied, 1)
            for g in range(NG):
                dve.wait_ge(x_in[g], 16)
                if g >= 4:
                    dve.wait_ge(dcol_done, g - 3)
                for t in range(g * HG, (g + 1) * HG):
                    last = nc.vector.tensor_tensor_reduce(
                        out=d_terms[:, t % (4 * HG), :], in0=x_sb[:, t, :], in1=w2_row[:], scale=1.0, scalar=0.0,
                        op0=ALU.mult, op1=ALU.add, accum_out=d_col[:, t:t + 1])
                last.then_inc(dcol_done, 1)

            def edges(i, c, h):
                r = NH * (c % 2) + h
                dve.wait_ge(adj_in[r], 16 * (PERIOD // 2) * i + 16 * (c // 2 + 1))
                nc.vector.scalar_tensor_tensor(
                    out=adj_sb[:, r, :].bitcast(fp32), in0=adj_sb[:, r, :], scalar=0.0,
                    in1=d_row[:, h * HC:(h + 1) * HC], op0=ALU.is_equal, op1=ALU.subtract).then_inc(u_done, 1)

            for g in range(NG // 2, NG):
                xg = x_sb[:, g * HG:(g + 1) * HG, :]
                nc.vector.tensor_tensor_reduce(out=sq_dve[:, g - NG // 2], in0=xg, in1=xg, scale=1.0, scalar=0.0,
                                               op0=ALU.mult, op1=ALU.add, accum_out=xsq[:, g:g + 1]
                                               ).then_inc(xsq_dve_done, 1)

            dve.wait_ge(drow_copied, NG // NH)
            edges(0, 0, 0)

            dve.wait_ge(xsq_dve_done, NG // 2)
            dve.wait_ge(xsq_act_done, NG // 2)
            nc.vector.tensor_reduce(xsq_max[:], xsq[:], AX.X, ALU.max).then_inc(xsq_read, 1)

            def s_columns(g):
                dve.wait_ge(h_ready, g + 1)
                hs = tp[g % RC][:].rearrange("p (t f) -> p t f", t=TP)[:, :, F]
                nc.vector.tensor_scalar(s_col[:, g * TP:(g + 1) * TP], hs, R * (1 - ALPHA) / BIG, None,
                                        ALU.mult).then_inc(s_copied, 1)

            s_columns(0)
            dve.wait_ge(magT_ready, 1)
            nc.vector.tensor_reduce(top2[:], acc[0][0:1, 0:2 * P].rearrange("o (m p) -> o m p", m=2), AX.X,
                                    ALU.max).then_inc(top_step, 1)
            dve.wait_ge(top_step, 1)
            nc.vector.tensor_scalar(bound[:], top2[:, 0:1], 1e-17, top2[:, 1:2], ALU.max, ALU.mult
                                    ).then_inc(top_step, 1)
            dve.wait_ge(top_step, 2)
            nc.vector.tensor_scalar(rpow2[:], bound[:], 1e-33, 1e33, ALU.max, ALU.min).then_inc(top_step, 1)
            dve.wait_ge(top_step, 3)
            nc.vector.tensor_scalar(pow2[:].bitcast(i32), rpow2[:].bitcast(i32), 0x7F800000, None,
                                    ALU.bitwise_and).then_inc(top_step, 1)
            dve.wait_ge(top_step, 4)
            nc.vector.reciprocal(rpow2[:], pow2[:]).then_inc(top_step, 1)
            dve.wait_ge(top_step, 5)
            nc.vector.tensor_scalar(sigma1[:], rpow2[:], HTOP / F ** 0.5, None, ALU.mult).then_inc(sigma1_ready, 1)
            dve.wait_ge(sigma_spread, 1)
            nc.vector.tensor_copy(sigma[:], acc[1][:, 0:1]).then_inc(sigma_ready, 1)

            def scores(i, c, h):
                r = NH * (c % 2) + h
                dve.wait_ge(u_done, NH * PERIOD * i + NH * c + h + 1)
                dve.wait_ge(relu_done, NH * PERIOD * i + NH * c + h + 1)
                if h:
                    dve.wait_ge(v_done, NH * PERIOD * i + NH * c + h)
                nc.vector.nop(nofuse=True)
                v = w[:, c % 2, h * HC:(h + 1) * HC]
                nc.vector.tensor_tensor_reduce(
                    out=v, in0=v, in1=adj_sb[:, r, :].bitcast(fp32), scale=1.0,
                    scalar=(wmax[:, c % 2, h - 1:h] if h else -3e38), op0=ALU.subtract, op1=ALU.max,
                    accum_out=wmax[:, c % 2, h:h + 1]).then_inc(v_done, 1)

            def row_max(i, c, ring_used=True):
                dve.wait_ge(v_done, NH * PERIOD * i + NH * (c + 1))
                if ring_used:
                    dve.wait_ge(exp_done, NH * PERIOD * i + NH * (c - 1))
                nc.vector.tensor_scalar(negmax[:, c % 2:c % 2 + 1], wmax[:, c % 2, NH - 1:NH], -BIG / R, SHIFT,
                                        ALU.mult, ALU.add).then_inc(negmax_done, 1)

            def low(i, c, k):
                dve.wait_ge(hi_done, NC * PERIOD * i + NC * c + k + 1)
                r = (NC * c + k + NP) % RC
                nc.vector.tensor_tensor(e_lo[:, r, :], tp[r][:], e_hi[:, r, :], ALU.subtract
                                        ).then_inc(lo_done, 1)

            dve.wait_ge(drow_copied, NG)
            dve.wait_ge(sigma_ready, 1)
            for g in range(NP):
                dve.wait_ge(hhi_done, g + 1)
                if g:
                    s_columns(g)
                nc.vector.scalar_tensor_tensor(
                    out=h_lo[:, g * TP:(g + 1) * TP, :],
                    in0=tp[g % RC][:].rearrange("p (t f) -> p t f", t=TP)[:, :, 0:F], scalar=sigma[:, 0:1],
                    in1=h_hi[:, g * TP:(g + 1) * TP, :], op0=ALU.mult, op1=ALU.subtract).then_inc(hlo_done, 1)
                if g == 1:
                    scores(0, 0, 0)
                elif g == 3:
                    edges(0, 0, 1)
                elif g == 5:
                    scores(0, 0, 1)
                    row_max(0, 0, False)
                elif g == 8:
                    edges(0, 1, 0)
                elif g == 10:
                    scores(0, 1, 0)
                elif g == 12:
                    edges(0, 1, 1)

            def tile(i, c):
                t = c if type(i) is int else None
                low(i, c, 0)
                if t is None or t + 1 < NT:
                    scores(i, c + 1, 1)
                    row_max(i, c + 1, t is None or t >= 1)
                low(i, c, 1)
                if t is None or t + 2 < NT:
                    edges(i, c + 2, 0)
                low(i, c, 2)
                if t is None or t + 2 < NT:
                    scores(i, c + 2, 0)
                low(i, c, 3)
                if t is None or t + 2 < NT:
                    edges(i, c + 2, 1)

            for t in range(PERIOD + 1):
                tile(0, t)
            with dve.Fori(1, LOOPS) as i:
                for c in range(1, PERIOD + 1):
                    tile(i, c)
            for t in PEELED:
                tile(0, t)

        @block.tensor
        def _(pe):
            pe.wait_ge(w_in, 16)
            pe.wait_ge(a2_ready, 1)
            for fb in range(KB):
                last = nc.tensor.matmul(acc[0][:, 0:F], a2_rep[:, fb, :], w_sb[:, fb, :],
                                        start=(fb == 0), stop=(fb == KB - 1))
            last.then_inc(w2_ready, 1)
            pe.wait_ge(a1_in, 16)
            for b in range(KB):
                for fb in range(KB):
                    nc.tensor.matmul(tp[2][:, b:b + 1], w_sb[:, fb, b * P:(b + 1) * P],
                                     a12[:, fb, 0:1], start=(fb == 0), stop=(fb == KB - 1))
            pe.wait_ge(ident_in, 16)
            for b in range(KB):
                for fb in range(KB):
                    last = nc.tensor.transpose(acc[1][:, b * F + fb * P:b * F + (fb + 1) * P],
                                               w_sb[:, fb, b * P:(b + 1) * P], ident[:])
            last.then_inc(wT_ready, 1)

            def d_row_group(g):
                pe.wait_ge(dcol_done, g + 1)
                if g >= 2:
                    pe.wait_ge(drow_copied, g - 1)
                for u in range(HG):
                    last = nc.tensor.matmul(acc[g % 2][:, u * P:(u + 1) * P],
                                            d_col[:, g * HG + u:g * HG + u + 1].broadcast_to([P, P]), ident[:],
                                            start=True, stop=True)
                last.then_inc(drow_ready, 1)

            for g in range(NG):
                pe.wait_ge(x_in[g], 16)
                if g == 2:
                    pe.wait_ge(wT_copied, 2)
                if g >= RC:
                    pe.wait_ge(xT_copied, g - RC + 1)
                for b in range(KB):
                    for u in range(HG):
                        last = nc.tensor.transpose(tp[g % RC][:, (b * HG + u) * P:(b * HG + u + 1) * P],
                                                   x_sb[:, g * HG + u, b * P:(b + 1) * P], ident[:])
                last.then_inc(xT_ready, 1)
                if g == 2:
                    pe.wait_ge(w2_copied, 1)
                if g >= 2:
                    d_row_group(g - 2)
            d_row_group(NG - 2)

            def h_pair(g):
                for u in range(TP):
                    t = g * TP + u
                    for b in range(KB):
                        last = nc.tensor.matmul(tp[g % RC][:, u * BANK:u * BANK + F + 1],
                                                xT[:, b, t * P:(t + 1) * P], wT[:, b, :],
                                                start=(b == 0), stop=(b == KB - 1))
                last.then_inc(h_ready, 1)

            pe.wait_ge(xT_copied, NG - 1)
            h_pair(0)
            d_row_group(NG - 1)
            pe.wait_ge(xT_copied, NG)
            h_pair(1)
            pe.wait_ge(wmax_ready, 1)
            pe.wait_ge(xroot_ready, 1)
            pe.wait_ge(drow_copied, NG)
            for m in range(2):
                last = nc.tensor.transpose(acc[0][0:1, m * P:(m + 1) * P], mag2[:, m:m + 1], ident[:])
            last.then_inc(magT_ready, 1)
            h_pair(2)
            pe.wait_ge(consts, 1)
            pe.wait_ge(sigma1_ready, 1)
            nc.tensor.matmul(acc[1][:, 0:1], ones[:], sigma1[:], start=True, stop=True).then_inc(sigma_spread, 1)
            for g in range(RC, NP):
                pe.wait_ge(hlo_done, g - RC + 1)
                h_pair(g)

            def flip(i, c, k, ring_used=True):
                if k % 2 == 0:
                    pe.wait_ge(exp_done, NH * PERIOD * i + NH * c + k // 2 + 1)
                if ring_used:
                    pe.wait_ge(lo_done, NC * PERIOD * i + NC * c + k - RC + 1)
                r = (NC * c + k + NP) % RC
                for b in range(CB):
                    j = k * CB + b
                    last = nc.tensor.transpose(tp[r][:, b * P:(b + 1) * P], w[:, c % 2, j * P:(j + 1) * P], ident[:])
                last.then_inc(tp_done, 1)

            def product(i, c, k, ring_used=True):
                r = (NC * c + k + NP) % RC
                sums = acc[c % 2][:, 0:F]
                if k == 0 and ring_used:
                    pe.wait_ge(scaled_done, PERIOD * i + c - 1)
                pe.wait_ge(lo_done, NC * PERIOD * i + NC * c + k + 1)
                for b in range(CB):
                    j = k * CB + b
                    hi = e_hi[:, r, b * P:(b + 1) * P]
                    nc.tensor.matmul(sums, hi, h_hi[:, j, :], start=(j == 0), stop=False)
                    nc.tensor.matmul(sums, hi, h_lo[:, j, :], start=False, stop=False)
                    last = nc.tensor.matmul(sums, e_lo[:, r, b * P:(b + 1) * P], h_hi[:, j, :],
                                            start=False, stop=(j == NT - 1))
                last.then_inc(prod_done, 1)

            def tile(i, c):
                t = c if type(i) is int else None
                for k in range(NC):
                    if k + 2 < NC:
                        flip(i, c, k + 2, t != 0 or k + 2 >= RC)
                    elif t is None or t + 1 < NT:
                        flip(i, c + 1, k + 2 - NC)
                    product(i, c, k, t is None or t >= 2)

            for k in range(2):
                pe.wait_ge(hlo_done, NP - RC + 1 + k)
                flip(0, 0, k, False)
            pe.wait_ge(hlo_done, NP)
            for t in range(PERIOD + 1):
                tile(0, t)
            with pe.Fori(1, LOOPS) as i:
                for c in range(1, PERIOD + 1):
                    tile(i, c)
            for t in PEELED:
                tile(0, t)


_INS = ['x', 'adj', 'L0_gnn_W', 'L0_gnn_a1', 'L0_gnn_a2']


def kernel(**inputs):
    import numpy as _np
    import concourse.bacc as _bacc
    from concourse import mybir as _mybir
    from concourse.bass_utils import run_bass_kernel_spmd as _run

    nc = _bacc.Bacc("TRN2", target_bir_lowering=False, num_devices=1)
    arrays, args = {}, []
    for name in _INS:
        a = _np.ascontiguousarray(inputs[name])
        arrays[f"in_{name}_dram"] = a
        args.append(nc.dram_tensor(f"in_{name}_dram", a.shape, _mybir.dt.from_np(a.dtype), kind="ExternalInput").ap())
    shape = inputs['x'].shape
    out = nc.dram_tensor("out_0_dram", shape, _mybir.dt.float32, kind="ExternalOutput").ap()
    identity = _np.eye(128, dtype=_np.float32)
    arrays["in_identity_dram"] = identity
    args.append(nc.dram_tensor("in_identity_dram", identity.shape, _mybir.dt.float32, kind="ExternalInput").ap())
    gat_layer(nc, *args, out)
    r = _run(nc, [arrays], core_ids=[0])
    return r.results[0]["out_0_dram"]
```
